# Optimizing a Trainium2 kernel written in Bass

```python
import numpy as np
import jax
import jax.numpy as jnp

def _softmax(x, axis=-1):
    return jax.nn.softmax(x, axis=axis)

def _gelu(x):
    return jax.nn.gelu(x, approximate=True)

def _silu(x):
    return jax.nn.silu(x)

def _sigmoid(x):
    return jax.nn.sigmoid(x)

def _layernorm(x, axis=-1, eps=1e-05):
    m = jnp.mean(x, axis=axis, keepdims=True)
    v = jnp.var(x, axis=axis, keepdims=True)
    return (x - m) / jnp.sqrt(v + eps)

def _scatter_add(tgt, idx, src, axis=0):
    return tgt.at[idx].add(src)

def _segment_sum(src, seg, n):
    return jax.ops.segment_sum(src, seg, n)
kernel_name = 'mk_adj_resnorm_d1_adj_r2_3b2b76'

def setup_inputs(seed: int=0):
    np.random.seed(seed)
    _w = jnp.asarray

    def _rec_inputs():
        import jax
        import jax.numpy as jnp
        _gk = jax.random.key(seed)
        x = -0.0002422 + 1 * jax.random.normal(jax.random.fold_in(_gk, 1), (128, 64, 512), jnp.float32)
        _a = jax.random.bernoulli(jax.random.fold_in(_gk, 2), 0.125, (128, 64, 64))
        _a = jnp.logical_or(_a, jnp.swapaxes(_a, -1, -2))
        _a = jnp.logical_or(_a, jnp.eye(64, dtype=bool))
        adj = _a.astype(jnp.int32)
        return (x, adj)
    x, adj = _rec_inputs()

    def _L0_gnn_setup():
        import jax, jax.numpy as jnp
        import numpy as np
        IN_DIM = 512
        OUT_DIM = 512
        BATCH = 128
        NUM_OBJS = 100
        key = jax.random.key(seed)
        k1, k2, k3, k4, k5 = jax.random.split(key, 5)
        stdv = 1.0 / np.sqrt(OUT_DIM)
        feature = jax.random.normal(k1, (BATCH, NUM_OBJS, IN_DIM), dtype=jnp.float32)
        graph = jax.random.randint(k2, (BATCH, NUM_OBJS, NUM_OBJS), 0, 2, dtype=jnp.int32)
        weight = jax.random.uniform(k3, (IN_DIM, OUT_DIM), dtype=jnp.float32, minval=-stdv, maxval=stdv)
        wq = jax.random.uniform(k4, (IN_DIM, OUT_DIM), dtype=jnp.float32, minval=-stdv, maxval=stdv)
        wk = jax.random.uniform(k5, (IN_DIM, OUT_DIM), dtype=jnp.float32, minval=-stdv, maxval=stdv)
        return {'feature': feature, 'graph': graph, 'weight': weight, 'wq': wq, 'wk': wk}
    _L0_gnn_all = _L0_gnn_setup()
    _L0_gnn_in = {k: v for k, v in _L0_gnn_all.items() if k in ('weight', 'wq', 'wk')}
    del _L0_gnn_all
    return {'x': x, 'adj': adj, 'L0_gnn_weight': _L0_gnn_in['weight'], 'L0_gnn_wq': _L0_gnn_in['wq'], 'L0_gnn_wk': _L0_gnn_in['wk']}

def reference(x, adj, L0_gnn_weight, L0_gnn_wq, L0_gnn_wk):
    import jax
    import jax.numpy as jnp

    def _L0_gnn_ref(feature, graph, weight, wq, wk):
        import jax, jax.numpy as jnp
        import numpy as np
        IN_DIM = 512
        OUT_DIM = 512
        BATCH = 128
        NUM_OBJS = 100
        output = jnp.einsum('bni,io->bno', feature, weight)
        q = jnp.einsum('bni,io->bno', feature, wq)
        k = jnp.einsum('bni,io->bno', feature, wk)
        alpha = jnp.einsum('bno,bmo->bnm', q, k)
        alpha = jnp.maximum(alpha, 0.0) * (graph != 0).astype(alpha.dtype)
        alpha = jax.nn.softmax(alpha, axis=1)
        return jnp.einsum('bnm,bmo->bno', alpha, output)
    x = _layernorm(x + _L0_gnn_ref(x, adj, L0_gnn_weight, L0_gnn_wq, L0_gnn_wk), axis=-1)
    return x

_drawn_inputs = setup_inputs


def setup_inputs(seed=0):
    import zlib

    import numpy as np

    out = dict(_drawn_inputs(seed))
    spreads = {}
    factors = {}
    for name, (base, spread) in spreads.items():
        noise = np.random.default_rng([zlib.crc32(name.encode()), seed]).standard_normal(out[name].shape)
        drawn = base * np.exp(spread * noise) if base else spread * noise
        out[name] = jnp.asarray(drawn.astype(out[name].dtype))
    for name, factor in factors.items():
        out[name] = (out[name] * factor).astype(out[name].dtype)
    return out
```

```python
from contextlib import ExitStack

import concourse.bass as bass
from concourse import mybir

ALU = mybir.AluOpType
ACT = mybir.ActivationFunctionType
AX_X = mybir.AxisListType.X
F32 = mybir.dt.float32
F32R = mybir.dt.float32r
I32 = mybir.dt.int32

P = 128
EPS = 1e-5
HIGH, LOW = 0, 1


def gnn_layer(nc: bass.Bass, x, adj, weight, wq, wk, out):
    B, N, D = x.shape
    C = D // P
    R = 4
    TB = P // N
    GB = R * TB
    ROWS = R * P
    G = B // GB
    Q = 32
    WB = GB // 2
    assert D == 512 and N == 64 and B % (2 * GB) == 0 and ROWS == 512 and C == R

    x_rows = x.rearrange("(g r b) n d -> g (b n) r d", r=R, b=TB)
    out_rows = out.rearrange("(g r b) n d -> g (b n) r d", r=R, b=TB)
    adj_blocks = adj.rearrange("(g b) (k a) (h c) -> g h a (b k) c", b=GB, a=Q, c=Q)

    with ExitStack() as ctx:
        def sb(name, shape, dt=F32):
            return ctx.enter_context(nc.sbuf_tensor(name, shape, dt))

        def sem(name):
            return ctx.enter_context(nc.semaphore(name))

        wq_raw = sb("wq_raw", [P, C, D])
        wk_raw = sb("wk_raw", [P, C, D])
        w_raw = sb("w_raw", [P, C, D])
        w_split = sb("w_split", [P, C, 2, D], F32R)
        m_split = sb("m_split", [P, C, 2, D], F32R)
        x_sb = sb("x_sb", [P, 2, R, D])
        xT = sb("xT", [P, 2, C, 2, ROWS], F32R)
        zT = sb("zT", [P, C, GB, 2, N], F32R)
        v = sb("v", [P, R, 2, D], F32R)
        wqT, wkT = zT[:].rearrange("p c b s n -> p c (b s n)").rearrange("p c (s d) -> p c s d", s=2), v
        y = sb("y", [P, 2, R, D])
        adj_sb = sb("adj_sb", [N, 2, GB, N], I32)
        linked = sb("linked", [N, GB, N])
        mask = sb("mask", [N, GB, N])
        halves = sb("halves", [P, GB, N])
        low_half = sb("low_half", [N, GB, N])
        logits = sb("logits", [N, GB, N])
        neg_max = sb("neg_max", [N, GB])
        total = sb("total", [N, GB])
        inverse = sb("inverse", [N, GB])
        probs = sb("probs", [N, R, TB, N])
        odd_high = sb("odd_high", [N, R, N], F32R)
        blocks = sb("blocks", [P, 2, R, P], F32R)
        stats = sb("stats", [P, R, 6])
        moments = sb("moments", [P, R, 2])
        var_eps = sb("var_eps", [P, R])
        rstd = sb("rstd", [P, R])
        mean_rstd = sb("mean_rstd", [P, R])
        shift = sb("shift", [P, R])
        eps = sb("eps", [P, R])
        minus_half = sb("minus_half", [P, R])
        minus_one = sb("minus_one", [P, R])
        identity = sb("identity", [P, P])

        product = [ctx.enter_context(nc.psum_tensor(f"product{i}", [P, D], F32)) for i in range(4)]
        square = [ctx.enter_context(nc.psum_tensor(f"square{i}", [P, ROWS], F32)) for i in range(2)]
        attended = [ctx.enter_context(nc.psum_tensor(f"attended{i}", [P, D], F32)) for i in range(2)]

        wq_loaded, wk_loaded, w_loaded = sem("wq_loaded"), sem("wk_loaded"), sem("w_loaded")
        x_loaded = [sem("x_loaded0"), sem("x_loaded1")]
        adj_loaded = [sem("adj_loaded0"), sem("adj_loaded1")]
        stored = [sem("stored0"), sem("stored1")]
        zeroed = sem("zeroed")
        constants_ready = sem("constants_ready")
        blocks_cleared = sem("blocks_cleared")
        w_high, w_low = sem("w_high"), sem("w_low")
        m_ready, m_high, m_low = sem("m_ready"), sem("m_high"), sem("m_low")
        turned = sem("turned")
        turned_high, turned_low = sem("turned_high"), sem("turned_low")
        z_ready, z_high, z_low = sem("z_ready"), sem("z_high"), sem("z_low")
        v_ready, v_high, v_low = sem("v_ready"), sem("v_high"), sem("v_low")
        logits_ready = sem("logits_ready")
        folded = sem("folded")
        moved = sem("moved")
        summed = sem("summed")
        compared = sem("compared")
        mask_ready = sem("mask_ready")
        masked = sem("masked")
        max_ready = sem("max_ready")
        shifted = sem("shifted")
        exp_ready = sem("exp_ready")
        total_ready = sem("total_ready")
        inverse_ready = sem("inverse_ready")
        probs_ready = sem("probs_ready")
        blocks_high, blocks_low = sem("blocks_high"), sem("blocks_low")
        out_ready = sem("out_ready")
        residual_added = sem("residual_added")
        stats_ready, moments_ready = sem("stats_ready"), sem("moments_ready")
        var_ready, rstd_ready, mean_ready = sem("var_ready"), sem("rstd_ready"), sem("mean_ready")
        shift_ready = sem("shift_ready")
        normalised = sem("normalised")

        WEIGHT_CHUNKS = 2 * C

        def steps(engine, step):
            step(0, 0, 0, first=True)
            with engine.Fori(0, (G - 2) // 2) as i:
                step(2 * i + 1, i, 1)
                step(2 * i + 2, i + 1, 0)
            step(G - 1, (G - 1) // 2, 1, last=True)

        block = ctx.enter_context(nc.Block())

        @block.sync
        def _(sp):
            for slot in range(2):
                sp.sem_inc(stored[slot], 16)
            sp.dma_start(wq_raw[:], wq.rearrange("(c p) d -> p c d", p=P)).then_inc(wq_loaded, 16)
            sp.dma_start(wk_raw[:], wk.rearrange("(c p) d -> p c d", p=P)).then_inc(wk_loaded, 16)

            def load(g, slot):
                sp.dma_start(x_sb[:, slot], x_rows[g]).then_inc(x_loaded[slot], 16)
                for h in range(2):
                    sp.dma_start(adj_sb[h * Q:(h + 1) * Q, slot].rearrange("a b (k c) -> a (b k) c", c=Q),
                                 adj_blocks[g, h]).then_inc(adj_loaded[slot], 16)

            load(0, 0)
            sp.dma_start(w_raw[:], weight.rearrange("(c p) d -> p c d", p=P)).then_inc(w_loaded, 16)

            def store(g, slot):
                sp.wait_ge(normalised, R * (g + 1))
                sp.dma_start(out_rows[g], y[:, slot]).then_inc(stored[slot], 16)

            def step(g, half, slot, first=False, last=False):
                if not last:
                    if not first:
                        sp.wait_ge(residual_added, R * g)
                        sp.wait_ge(mask_ready, g)
                    load(g + 1, 1 - slot)
                if not first:
                    store(g - 1, 1 - slot)

            steps(sp, step)
            store(G - 1, 1)
            for slot in range(2):
                sp.wait_ge(stored[slot], 16 * (1 + G // 2))

        @block.tensor
        def _(pe):
            def transpose(src, c, bank):
                for r in range(R):
                    last = nc.tensor.transpose(bank[:, r * P:(r + 1) * P], src[:, r, c * P:(c + 1) * P],
                                               identity[:])
                last.then_inc(turned, 1)

            def split_product(bank, stationary, moving):
                for c in range(C):
                    for s, t in ((HIGH, HIGH), (HIGH, LOW), (LOW, HIGH)):
                        mm = nc.tensor.matmul(bank[:], stationary(c, s), moving(c, t),
                                              start=(c == 0 and s == t), stop=(c == C - 1 and s == LOW))
                return mm

            pe.wait_ge(constants_ready, 1)
            for n in range(WEIGHT_CHUNKS + C):
                src, loaded = ((wq_raw, wq_loaded), (wk_raw, wk_loaded), (x_sb[:, 0], x_loaded[0]))[n // C]
                if n % C == 0:
                    pe.wait_ge(loaded, 16)
                if n >= 2:
                    pe.wait_ge(turned_low, n - 1)
                transpose(src, n % C, square[n % 2])
            for j in range(C):
                split_product(product[j], lambda c, s: wkT[:, c, s, j * P:(j + 1) * P],
                              lambda c, s: wqT[:, c, s, :]).then_inc(m_ready, 1)

            def z_chunk(g, slot, i, first):
                if i == 0:
                    pe.wait_ge(turned_low, WEIGHT_CHUNKS + C * (g + 1))
                if first:
                    pe.wait_ge(m_low, C)
                else:
                    pe.wait_ge(v_low, R * g - R + i + 1)
                split_product(product[i], lambda c, s: m_split[:, c, s, i * P:(i + 1) * P],
                              lambda c, s: xT[:, slot, c, s, :]).then_inc(z_ready, 1)

            def attend(g, r):
                if r == 0:
                    pe.wait_ge(v_low, R * g + R)
                    pe.wait_ge(blocks_high, 3 * g + 3)
                    pe.wait_ge(blocks_low, 2 * g + 2)
                if r >= 2:
                    pe.wait_ge(residual_added, R * g + r - 1)
                for s, t in ((HIGH, HIGH), (HIGH, LOW), (LOW, HIGH)):
                    mm = nc.tensor.matmul(attended[r % 2][:], blocks[:, s, r, :], v[:, r, t, :],
                                          start=(s == t), stop=(s == LOW))
                mm.then_inc(out_ready, 1)

            def v_tile(g, slot, r, first):
                pe.wait_ge(z_low, C * g + r + 1)
                if first and r == 0:
                    pe.wait_ge(w_low, 1)
                split_product(product[r], lambda c, s: xT[:, slot, c, s, r * P:(r + 1) * P],
                              lambda c, s: w_split[:, c, s, :]).then_inc(v_ready, 1)

            def logits_of(g, slot):
                pe.wait_ge(z_low, C * g + C)
                for k in range(2):
                    for b in range(WB):
                        rows = slice((k * WB + b) * N, (k * WB + b + 1) * N)
                        for c in range(C):
                            mm = nc.tensor.matmul(square[k][:, b * P:(b + 1) * P], zT[:, c, k * WB + b].rearrange("p s n -> p (s n)"),
                                                  xT[:, slot, c, :, rows], start=(c == 0), stop=(c == C - 1))
                    mm.then_inc(logits_ready, 1)

            def transpose_next(g, half, slot):
                pe.wait_ge(x_loaded[1 - slot], 16 * (half + slot + 1))
                for c in range(C):
                    if c < 2:
                        pe.wait_ge(folded, 2 * g + c + 1)
                    else:
                        pe.wait_ge(turned_low, WEIGHT_CHUNKS + C * (g + 1) + c - 1)
                    transpose(x_sb[:, 1 - slot], c, square[c % 2])

            def step(g, half, slot, first=False, last=False):
                for i in range(C):
                    z_chunk(g, slot, i, first)
                    if not first and i in (1, 2):
                        attend(g - 1, 2 * i - 2)
                        attend(g - 1, 2 * i - 1)
                v_tile(g, slot, 0, first)
                logits_of(g, slot)
                v_tile(g, slot, 1, first)
                v_tile(g, slot, 2, first)
                if not last:
                    transpose_next(g, half, slot)
                v_tile(g, slot, 3, first)

            steps(pe, step)
            for r in range(R):
                attend(G - 1, r)

        @block.scalar
        def _(act):
            def turn_high(n, dst):
                act.wait_ge(turned, n + 1)
                nc.scalar.copy(dst[:, n % C, HIGH, :], square[n % 2][:]).then_inc(turned_high, 1)

            for n in range(WEIGHT_CHUNKS + C):
                turn_high(n, (wqT, wkT, xT[:, 0])[n // C])
            act.wait_ge(w_loaded, 16)
            nc.scalar.copy(w_split[:, :, HIGH, :], w_raw[:]).then_inc(w_high, 1)
            for j in range(C):
                act.wait_ge(m_ready, j + 1)
                nc.scalar.copy(m_split[:, j, HIGH, :], product[j][:]).then_inc(m_high, 1)

            def z_part(g, i):
                act.wait_ge(z_ready, C * g + i + 1)
                nc.scalar.copy(zT[:, i, :, HIGH, :], product[i][:].rearrange("p (b n) -> p b n", n=N)).then_inc(z_high, 1)

            def v_part(g, r):
                act.wait_ge(v_ready, R * g + r + 1)
                nc.scalar.copy(v[:, r, HIGH, :], product[r][:]).then_inc(v_high, 1)

            def normalise(g, slot):
                act.wait_ge(shift_ready, g + 1)
                for r in range(R):
                    nc.scalar.activation(y[:, slot, r, :], y[:, slot, r, :], ACT.Identity, bias=shift[:, r:r + 1],
                                         scale=rstd[:, r:r + 1]).then_inc(normalised, 1)

            def step(g, half, slot, first=False, last=False):
                if not first:
                    act.wait_ge(logits_ready, 2 * g)
                for i in range(C):
                    z_part(g, i)
                if not first:
                    normalise(g - 1, 1 - slot)
                    act.wait_ge(out_ready, R * g)
                v_part(g, 0)
                if not first:
                    act.wait_ge(summed, g)
                for k in range(2):
                    act.wait_ge(folded, 2 * g + k + 1)
                    nc.scalar.copy(low_half[:, k * WB:(k + 1) * WB, :],
                                   halves[N:P, k * WB:(k + 1) * WB, :]).then_inc(moved, 1)
                v_part(g, 1)
                v_part(g, 2)
                if not last:
                    for c in range(C):
                        act.wait_ge(turned, WEIGHT_CHUNKS + C * (g + 1) + c + 1)
                        nc.scalar.copy(xT[:, 1 - slot, c, HIGH, :], square[c % 2][:]).then_inc(turned_high, 1)
                act.wait_ge(shifted, g + 1)
                nc.scalar.activation(logits[:], logits[:], ACT.Exp).then_inc(exp_ready, 1)
                v_part(g, 3)
                if first:
                    act.wait_ge(blocks_cleared, 1)
                act.wait_ge(probs_ready, g + 1)
                nc.scalar.copy(blocks[0:N, HIGH, :, 0:N], probs[:, :, 0, :]).then_inc(blocks_high, 1)
                nc.scalar.copy(odd_high[:], probs[:, :, 1, :]).then_inc(blocks_high, 1)
                nc.scalar.copy(blocks[N:P, HIGH, :, N:P], probs[:, :, 1, :]).then_inc(blocks_high, 1)

            steps(act, step)
            normalise(G - 1, 1)

        @block.vector
        def _(dve):
            def low_part(split, bank):
                return nc.vector.tensor_tensor(split[:, LOW, :], bank[:], split[:, HIGH, :].bitcast(F32), ALU.subtract)

            for n in range(WEIGHT_CHUNKS + C):
                dve.wait_ge(turned_high, n + 1)
                low_part((wqT, wkT, xT[:, 0])[n // C][:, n % C], square[n % 2]).then_inc(turned_low, 1)
            dve.wait_ge(w_high, 1)
            nc.vector.tensor_tensor(w_split[:, :, LOW, :], w_raw[:], w_split[:, :, HIGH, :].bitcast(F32),
                                    ALU.subtract).then_inc(w_low, 1)
            for j in range(C):
                dve.wait_ge(m_high, j + 1)
                low_part(m_split[:, j], product[j]).then_inc(m_low, 1)

            def z_part(g, i):
                dve.wait_ge(z_high, C * g + i + 1)
                nc.vector.tensor_tensor(zT[:, i, :, LOW, :], product[i][:].rearrange("p (b n) -> p b n", n=N),
                                        zT[:, i, :, HIGH, :].bitcast(F32), ALU.subtract).then_inc(z_low, 1)

            def v_part(g, r):
                dve.wait_ge(v_high, R * g + r + 1)
                low_part(v[:, r], product[r]).then_inc(v_low, 1)

            def residual(g, slot, r):
                dve.wait_ge(out_ready, R * g + r + 1)
                nc.vector.tensor_tensor(y[:, slot, r, :], attended[r % 2][:], x_sb[:, slot, r, :],
                                        ALU.add).then_inc(residual_added, 1)
                dve.wait_ge(residual_added, R * g + r + 1)
                nc.vector.bn_stats(stats[:, r, :], y[:, slot, r, :]).then_inc(stats_ready, 1)

            def aggregate():
                for r in range(R):
                    nc.vector.bn_aggr(moments[:, r, :], stats[:, r, :]).then_inc(moments_ready, 1)

            def make_mask(half, slot, g):
                dve.wait_ge(adj_loaded[slot], 32 * (half + 1))
                nc.vector.tensor_scalar(linked[:], adj_sb[:, slot], 0.0, None, ALU.not_equal).then_inc(compared, 1)
                dve.wait_ge(compared, g + 1)
                nc.vector.transpose(mask[:].rearrange("m b n -> m (b n)"),
                                    linked[:].rearrange("m b n -> m (b n)")).then_inc(mask_ready, 1)

            def fold(g):
                for k in range(2):
                    dve.wait_ge(logits_ready, 2 * g + k + 1)
                    nc.vector.tensor_reduce(halves[:, k * WB:(k + 1) * WB, :],
                                            square[k][:].rearrange("p (b s n) -> p b n s", s=2, n=N),
                                            AX_X, ALU.add).then_inc(folded, 1)

            def mask_logits(g):
                dve.wait_ge(moved, 2 * g + 2)
                dve.wait_ge(folded, 2 * g + 2)
                nc.vector.tensor_tensor(logits[:], halves[0:N], low_half[:], ALU.add).then_inc(summed, 1)
                dve.wait_ge(summed, g + 1)
                dve.wait_ge(mask_ready, g + 1)
                nc.vector.scalar_tensor_tensor(out=logits[:], in0=logits[:], scalar=0.0, in1=mask[:],
                                               op0=ALU.max, op1=ALU.mult).then_inc(masked, 1)

            def subtract_max(g):
                dve.wait_ge(masked, g + 1)
                nc.vector.tensor_reduce(neg_max[:], logits[:], AX_X, ALU.max, negate=True).then_inc(max_ready, 1)
                dve.wait_ge(max_ready, g + 1)
                nc.vector.tensor_tensor(logits[:], logits[:], neg_max[:].unsqueeze(2).broadcast_to([N, GB, N]),
                                        ALU.add).then_inc(shifted, 1)

            def softmax(g, first):
                dve.wait_ge(exp_ready, g + 1)
                nc.vector.tensor_reduce(total[:], logits[:], AX_X, ALU.add).then_inc(total_ready, 1)
                dve.wait_ge(total_ready, g + 1)
                nc.vector.reciprocal(inverse[:], total[:]).then_inc(inverse_ready, 1)
                dve.wait_ge(inverse_ready, g + 1)
                if not first:
                    dve.wait_ge(blocks_high, 3 * g)
                nc.vector.tensor_tensor(probs[:].rearrange("m r t n -> m (r t) n"), logits[:],
                                        inverse[:].unsqueeze(2).broadcast_to([N, GB, N]),
                                        ALU.mult).then_inc(probs_ready, 1)

            def blocks_part(g):
                dve.wait_ge(probs_ready, g + 1)
                for t, high in ((0, blocks[0:N, HIGH, :, 0:N]), (1, odd_high[:])):
                    dve.wait_ge(blocks_high, 3 * g + t + 1)
                    nc.vector.tensor_tensor(blocks[t * N:(t + 1) * N, LOW, :, t * N:(t + 1) * N], probs[:, :, t, :],
                                            high.bitcast(F32), ALU.subtract).then_inc(blocks_low, 1)

            def step(g, half, slot, first=False, last=False):
                if not first:
                    dve.wait_ge(stored[1 - slot], 16 * (half + slot))
                z_part(g, 0)
                z_part(g, 1)
                if not first:
                    residual(g - 1, 1 - slot, 0)
                    residual(g - 1, 1 - slot, 1)
                z_part(g, 2)
                if not first:
                    residual(g - 1, 1 - slot, 2)
                    residual(g - 1, 1 - slot, 3)
                    dve.wait_ge(stats_ready, R * g)
                z_part(g, 3)
                if not first:
                    aggregate()
                make_mask(half, slot, g)
                v_part(g, 0)
                fold(g)
                v_part(g, 1)
                mask_logits(g)
                v_part(g, 2)
                subtract_max(g)
                if not last:
                    for c in range(C):
                        dve.wait_ge(turned_high, WEIGHT_CHUNKS + C * (g + 1) + c + 1)
                        low_part(xT[:, 1 - slot, c], square[c % 2]).then_inc(turned_low, 1)
                softmax(g, first)
                v_part(g, 3)
                blocks_part(g)

            steps(dve, step)
            dve.wait_ge(stored[1], 16 * (G // 2))
            for r in range(R):
                residual(G - 1, 1, r)
            dve.wait_ge(stats_ready, R * G)
            aggregate()

        @block.gpsimd
        def _(pool):
            nc.gpsimd.memset(identity[:], 0.0).then_inc(zeroed, 1)
            pool.wait_ge(zeroed, 1)
            nc.gpsimd.affine_select(out=identity[:], in_=identity[:], compare_op=ALU.not_equal, fill=1.0, base=0,
                                    pattern=[[-1, P]], channel_multiplier=1).then_inc(constants_ready, 1)
            for constant, value in ((eps, EPS), (minus_half, -0.5), (minus_one, -1.0)):
                nc.gpsimd.memset(constant[:], value).then_inc(constants_ready, 1)
            nc.gpsimd.memset(blocks[:].bitcast(F32), 0.0).then_inc(blocks_cleared, 1)

            def scale_and_shift(g):
                pool.wait_ge(moments_ready, R * g + R)
                nc.gpsimd.tensor_tensor(var_eps[:], moments[:, :, 1], eps[:], ALU.add).then_inc(var_ready, 1)
                pool.wait_ge(var_ready, g + 1)
                pool.wait_ge(v_high, R * g + 1)
                nc.gpsimd.tensor_tensor(rstd[:], var_eps[:], minus_half[:], ALU.pow).then_inc(rstd_ready, 1)
                pool.wait_ge(rstd_ready, g + 1)
                nc.gpsimd.tensor_tensor(mean_rstd[:], moments[:, :, 0], rstd[:], ALU.mult).then_inc(mean_ready, 1)
                pool.wait_ge(mean_ready, g + 1)
                nc.gpsimd.tensor_tensor(shift[:], mean_rstd[:], minus_one[:], ALU.mult).then_inc(shift_ready, 1)

            pool.wait_ge(constants_ready, 4)

            def step(g, half, slot, first=False, last=False):
                if not first:
                    scale_and_shift(g - 1)

            steps(pool, step)
            scale_and_shift(G - 1)


_INS = ["x", "adj", "L0_gnn_weight", "L0_gnn_wq", "L0_gnn_wk"]


def kernel(**inputs):
    import numpy as _np
    import concourse.bacc as _bacc
    from concourse import mybir as _mybir
    from concourse.bass_utils import run_bass_kernel_spmd as _run

    nc = _bacc.Bacc("TRN2", target_bir_lowering=False, num_devices=1)
    arrays, args = {}, []
    for name in _INS:
        a = _np.ascontiguousarray(inputs[name])
        arrays[f"in_{name}"] = a
        args.append(nc.dram_tensor(f"in_{name}", a.shape, _mybir.dt.from_np(a.dtype), kind="ExternalInput").ap())
    result = nc.dram_tensor("out", inputs["x"].shape, _mybir.dt.from_np(_np.dtype("float32")),
                            kind="ExternalOutput").ap()
    gnn_layer(nc, *args, result)
    return _run(nc, [arrays], core_ids=[0]).results[0]["out"]
```

```python
from contextlib import ExitStack

import concourse.bass as bass
from concourse import mybir

ALU = mybir.AluOpType
ACT = mybir.ActivationFunctionType
AX_X = mybir.AxisListType.X
F32 = mybir.dt.float32
F32R = mybir.dt.float32r
I32 = mybir.dt.int32

P = 128
Q = 32
EPS = 1e-5
HIGH, LOW = 0, 1


def gnn_layer(nc: bass.Bass, x, adj, weight, wq, wk, out):
    B, N, D = x.shape
    C = D // P
    R = 4
    TB = P // N
    GB = R * TB
    ROWS = R * P
    G = B // GB
    H = C // 2
    assert D == 512 and N == 64 and B % (2 * GB) == 0 and ROWS == D and P // Q == C

    x_rows = x.rearrange("(g r b) n d -> g (b n) r d", r=R, b=TB)
    out_rows = out.rearrange("(g r b) n d -> g (b n) r d", r=R, b=TB)
    x_cols = x.rearrange("(g b) (k a) (q f) -> g q a (b k) f", b=GB, a=Q, f=P)
    wq_cols = wq.rearrange("(k a) (q f) -> q a k f", a=Q, f=P)
    wk_cols = wk.rearrange("(k a) (q f) -> q a k f", a=Q, f=P)
    w_rows = weight.rearrange("(q b e) d -> q e b d", q=C, e=Q)
    adj_blocks = adj.rearrange("(r t) (k a) (h c) -> t h k a r c", t=TB, a=Q, c=Q)

    with ExitStack() as ctx:
        def sb(name, shape, dt=F32):
            return ctx.enter_context(nc.sbuf_tensor(name, shape, dt))

        def sem(name):
            return ctx.enter_context(nc.semaphore(name))

        w_split = sb("w_split", [P, C, 2, D], F32R)
        m_split = sb("m_split", [P, C, 2, D], F32R)
        xT = sb("xT", [P, 2, C, 2, ROWS], F32R)
        zT = sb("zT", [P, C, 2, ROWS], F32R)
        v = sb("v", [P, R, 2, D], F32R)
        blocks = sb("blocks", [P, 2, R, P], F32R)
        x_sb = sb("x_sb", [P, 2, R, D])
        x_quads = sb("x_quads", [P, ROWS // Q, P])
        halfT = sb("halfT", [P, 2, H, ROWS])
        y = sb("y", [P, 2, R, D])
        w_raw = x_sb[:, 1]
        wk_quads = y[:, 0].rearrange("p r (s f) -> p (r s) f", f=P)
        wq_quads = y[:, 1].rearrange("p r (s f) -> p (r s) f", f=P)
        wkT, wqT = xT[:, 1], zT[:]
        adj_sb = sb("adj_sb", [P, G * R, N], I32)
        linked = sb("linked", [P, R, N])
        mask = sb("mask", [P, R, N])
        logits = sb("logits", [P, R, N])
        neg_max = sb("neg_max", [P, R])
        total = sb("total", [P, R])
        inverse = sb("inverse", [P, R])
        probs = sb("probs", [P, R, N])
        stats = sb("stats", [P, R, 6])
        moments = sb("moments", [P, R, 2])
        var_eps = sb("var_eps", [P, R])
        rstd = sb("rstd", [P, R])
        mean_rstd = sb("mean_rstd", [P, R])
        shift = sb("shift", [P, R])
        eps = sb("eps", [P, R])
        minus_half = sb("minus_half", [P, R])
        minus_one = sb("minus_one", [P, R])

        product = [ctx.enter_context(nc.psum_tensor(f"product{i}", [P, D], F32)) for i in range(4)]
        raw_logits = ctx.enter_context(nc.psum_tensor("raw_logits", [P, R, 2, P], F32))
        attended = [ctx.enter_context(nc.psum_tensor(f"attended{i}", [P, D], F32)) for i in range(2)]

        x_quads_loaded, wk_loaded, wq_loaded = sem("x_quads_loaded"), sem("wk_loaded"), sem("wq_loaded")
        w_loaded, adj_loaded = sem("w_loaded"), sem("adj_loaded")
        x_loaded = [sem("x_loaded0"), sem("x_loaded1")]
        stored = [sem("stored0"), sem("stored1")]
        blocks_cleared = sem("blocks_cleared")
        constants_ready = sem("constants_ready")
        turned = sem("turned")
        turned_high, turned_low = sem("turned_high"), sem("turned_low")
        w_high, w_low = sem("w_high"), sem("w_low")
        m_ready, m_high, m_low = sem("m_ready"), sem("m_high"), sem("m_low")
        z_ready, z_high, z_low = sem("z_ready"), sem("z_high"), sem("z_low")
        v_ready, v_high, v_low = sem("v_ready"), sem("v_high"), sem("v_low")
        logits_ready = sem("logits_ready")
        folded = sem("folded")
        compared, mask_ready, masked = sem("compared"), sem("mask_ready"), sem("masked")
        max_ready, shifted = sem("max_ready"), sem("shifted")
        exp_ready, total_ready, inverse_ready = sem("exp_ready"), sem("total_ready"), sem("inverse_ready")
        probs_ready = sem("probs_ready")
        blocks_high, blocks_low = sem("blocks_high"), sem("blocks_low")
        out_ready = sem("out_ready")
        residual_added = sem("residual_added")
        stats_ready, moments_ready = sem("stats_ready"), sem("moments_ready")
        var_ready, rstd_ready, mean_ready = sem("var_ready"), sem("rstd_ready"), sem("mean_ready")
        shift_ready = sem("shift_ready")
        normalised = sem("normalised")

        SETUP = [(x_quads[:], x_quads_loaded, xT[:, 0]), (wk_quads, wk_loaded, wkT), (wq_quads, wq_loaded, wqT)]

        def halves_before(g):
            return 2 * (len(SETUP) - 1) + 2 * g

        EARLY = 3

        def steps(engine, step):
            step(0, 0, 0, first=True)
            with engine.Fori(0, (G - 2) // 2) as i:
                step(2 * i + 1, i, 1)
                step(2 * i + 2, i + 1, 0)
            step(G - 1, (G - 1) // 2, 1, last=True)

        block = ctx.enter_context(nc.Block())

        @block.sync
        def _(sp):
            def load_quads(dst, src, loaded):
                for q in range(C):
                    sp.dma_start(dst[q * Q:(q + 1) * Q], src[q]).then_inc(loaded, 16)

            for slot in range(2):
                sp.sem_inc(stored[slot], 16)
            load_quads(x_quads[:], x_cols[0], x_quads_loaded)
            load_quads(w_raw, w_rows, w_loaded)
            load_quads(wk_quads, wk_cols, wk_loaded)
            load_quads(wq_quads, wq_cols, wq_loaded)
            for t in range(TB):
                for h in range(N // Q):
                    for k in range(N // Q):
                        sp.dma_start(adj_sb[(t * 2 + h) * Q:(t * 2 + h + 1) * Q, :, k * Q:(k + 1) * Q],
                                     adj_blocks[t, h, k]).then_inc(adj_loaded, 16)

            def store(g, slot):
                sp.wait_ge(normalised, R * (g + 1))
                sp.dma_start(out_rows[g], y[:, slot]).then_inc(stored[slot], 16)

            def step(g, half, slot, first=False, last=False):
                if not last:
                    sp.wait_ge(turned, 2 if first else halves_before(g) + 2)
                    load_quads(x_quads[:], x_cols[g + 1], x_quads_loaded)
                if slot == 1 and not first:
                    sp.wait_ge(w_low, 1)
                sp.dma_start(x_sb[:, slot], x_rows[g]).then_inc(x_loaded[slot], 16)
                if not first:
                    store(g - 1, 1 - slot)

            steps(sp, step)
            store(G - 1, 1)
            for slot in range(2):
                sp.wait_ge(stored[slot], 16 * (1 + G // 2))

        @block.tensor
        def _(pe):
            def split_product(bank, stationary, moving):
                for c in range(C):
                    for s, t in ((HIGH, HIGH), (HIGH, LOW), (LOW, HIGH)):
                        mm = nc.tensor.matmul(bank[:], stationary(c, s), moving(c, t),
                                              start=(c == 0 and s == t), stop=(c == C - 1 and s == LOW))
                return mm

            def z_chunk(slot, i):
                split_product(product[i], lambda c, s: m_split[:, c, s, i * P:(i + 1) * P],
                              lambda c, s: xT[:, slot, c, s, :]).then_inc(z_ready, 1)

            def v_tile(slot, r):
                split_product(product[r], lambda c, s: xT[:, slot, c, s, r * P:(r + 1) * P],
                              lambda c, s: w_split[:, c, s, :]).then_inc(v_ready, 1)

            def logits_of(g, slot):
                pe.wait_ge(z_low, C * g + C)
                for r in range(R):
                    rows = slice(r * P, (r + 1) * P)
                    for c in range(C):
                        nc.tensor.matmul(raw_logits[:, r], zT[:, c, HIGH, rows], xT[:, slot, c, :, rows],
                                         start=(c == 0), stop=False)
                        mm = nc.tensor.matmul(raw_logits[:, r, HIGH], zT[:, c, LOW, rows],
                                              xT[:, slot, c, HIGH, rows], start=False, stop=(c == C - 1))
                mm.then_inc(logits_ready, 1)

            def attend(g, r):
                if r == 0:
                    pe.wait_ge(v_low, R * g + R)
                    pe.wait_ge(blocks_high, 2 * g + 2)
                    pe.wait_ge(blocks_low, 2 * g + 2)
                if r >= 2:
                    pe.wait_ge(residual_added, R * g + r - 1)
                for s, t in ((HIGH, HIGH), (HIGH, LOW), (LOW, HIGH)):
                    mm = nc.tensor.matmul(attended[r % 2][:], blocks[:, s, r, :], v[:, r, t, :],
                                          start=(s == t), stop=(s == LOW))
                mm.then_inc(out_ready, 1)

            pe.wait_ge(w_low, 1)
            pe.wait_ge(turned_low, 2)
            for r in range(EARLY):
                v_tile(0, r)
            pe.wait_ge(turned_low, 2 * len(SETUP))
            for j in range(C):
                if j < EARLY:
                    pe.wait_ge(v_low, j + 1)
                split_product(product[j], lambda c, s: wkT[:, c, s, j * P:(j + 1) * P],
                              lambda c, s: wqT[:, c, s, :]).then_inc(m_ready, 1)
            pe.wait_ge(m_low, C)

            def step(g, half, slot, first=False, last=False):
                if not first:
                    pe.wait_ge(turned_low, halves_before(g) + 2)
                for i in range(C):
                    if not first:
                        pe.wait_ge(v_low, R * g - R + i + 1)
                    z_chunk(slot, i)
                    if not first and i in (1, 2):
                        attend(g - 1, 2 * i - 2)
                        attend(g - 1, 2 * i - 1)
                for r in range(EARLY if first else 0, R):
                    if r == (EARLY if first else 1):
                        logits_of(g, slot)
                    pe.wait_ge(z_low, C * g + r + 1)
                    v_tile(slot, r)

            steps(pe, step)
            for r in range(R):
                attend(G - 1, r)

        @block.scalar
        def _(act):
            def turn_high(u, h, dst):
                act.wait_ge(turned, u + 1)
                nc.scalar.copy(dst[:, h * H:(h + 1) * H, HIGH, :], halfT[:, h]).then_inc(turned_high, 1)

            def m_part(j):
                act.wait_ge(m_ready, j + 1)
                nc.scalar.copy(m_split[:, j, HIGH, :], product[j][:]).then_inc(m_high, 1)

            def z_part(g, i):
                act.wait_ge(z_ready, C * g + i + 1)
                nc.scalar.copy(zT[:, i, HIGH, :], product[i][:]).then_inc(z_high, 1)

            def v_part(g, r):
                act.wait_ge(v_ready, R * g + r + 1)
                nc.scalar.copy(v[:, r, HIGH, :], product[r][:]).then_inc(v_high, 1)

            def normalise(g, slot):
                act.wait_ge(shift_ready, g + 1)
                for r in range(R):
                    nc.scalar.activation(y[:, slot, r, :], y[:, slot, r, :], ACT.Identity, bias=shift[:, r:r + 1],
                                         scale=rstd[:, r:r + 1]).then_inc(normalised, 1)

            for h in range(2):
                turn_high(h, h, xT[:, 0])
            act.wait_ge(w_loaded, 16 * C)
            nc.scalar.copy(w_split[:, :, HIGH, :], w_raw).then_inc(w_high, 1)
            for u in range(2, 2 * len(SETUP)):
                turn_high(u, u % 2, SETUP[u // 2][2])
            for r in range(EARLY):
                v_part(0, r)
            for j in range(C):
                m_part(j)

            def step(g, half, slot, first=False, last=False):
                if not first:
                    act.wait_ge(logits_ready, g)
                    act.wait_ge(v_ready, R * g)
                for i in range(C):
                    z_part(g, i)
                    if not last and i in (1, 2):
                        turn_high(halves_before(g + 1) + i - 1, i - 1, xT[:, 1 - slot])
                if not first:
                    normalise(g - 1, 1 - slot)
                    act.wait_ge(out_ready, R * g)
                    v_part(g, 0)
                    v_part(g, 1)
                act.wait_ge(shifted, g + 1)
                nc.scalar.activation(logits[:], logits[:], ACT.Exp).then_inc(exp_ready, 1)
                if not first:
                    v_part(g, 2)
                else:
                    act.wait_ge(blocks_cleared, 1)
                act.wait_ge(probs_ready, g + 1)
                for t in range(TB):
                    nc.scalar.copy(blocks[t * N:(t + 1) * N, HIGH, :, t * N:(t + 1) * N],
                                   probs[t * N:(t + 1) * N]).then_inc(blocks_high, 1)
                v_part(g, 3)

            steps(act, step)
            normalise(G - 1, 1)

        @block.vector
        def _(dve):
            def turn(u, h, src):
                if u >= 2:
                    dve.wait_ge(turned_low, u - 1)
                nc.vector.transpose(halfT[:, h].rearrange("p b (k a) -> p b k a", a=Q),
                                    src.rearrange("p k (b c) -> p b k c", c=Q)[:, h * H:(h + 1) * H]).then_inc(turned, 1)

            def turn_weight(u, h, src):
                dve.wait_ge(turned_low, u - 1)
                for b in range(H):
                    last = nc.vector.transpose(halfT[:, h, b].rearrange("p (f q a) -> p q f a", q=C, a=Q),
                                               src.rearrange("p (q f) (b c) -> p b q f c", q=C, c=Q)[:, h * H + b])
                last.then_inc(turned, 1)

            def turn_low(u, h, dst):
                dve.wait_ge(turned_high, u + 1)
                dve.wait_ge(turned, u + 1)
                nc.vector.tensor_tensor(dst[:, h * H:(h + 1) * H, LOW, :], halfT[:, h],
                                        dst[:, h * H:(h + 1) * H, HIGH, :].bitcast(F32),
                                        ALU.subtract).then_inc(turned_low, 1)

            def low_part(split, bank):
                return nc.vector.tensor_tensor(split[:, LOW, :], bank[:], split[:, HIGH, :].bitcast(F32), ALU.subtract)

            def m_part(j):
                dve.wait_ge(m_high, j + 1)
                low_part(m_split[:, j], product[j]).then_inc(m_low, 1)

            def z_part(g, i):
                dve.wait_ge(z_high, C * g + i + 1)
                low_part(zT[:, i], product[i]).then_inc(z_low, 1)

            def v_part(g, r):
                dve.wait_ge(v_high, R * g + r + 1)
                low_part(v[:, r], product[r]).then_inc(v_low, 1)

            def residual(g, slot, r):
                dve.wait_ge(out_ready, R * g + r + 1)
                nc.vector.tensor_tensor(y[:, slot, r, :], attended[r % 2][:], x_sb[:, slot, r, :],
                                        ALU.add).then_inc(residual_added, 1)
                dve.wait_ge(residual_added, R * g + r + 1)
                nc.vector.bn_stats(stats[:, r, :], y[:, slot, r, :]).then_inc(stats_ready, 1)

            def aggregate():
                for r in range(R):
                    nc.vector.bn_aggr(moments[:, r, :], stats[:, r, :]).then_inc(moments_ready, 1)

            def make_mask(g):
                nc.vector.tensor_scalar(linked[:], adj_sb[:, bass.ts(g, R)], 0.0, None,
                                        ALU.not_equal).then_inc(compared, 1)
                dve.wait_ge(compared, g + 1)
                nc.vector.transpose(mask[:].rearrange("m r n -> m (r n)"),
                                    linked[:].rearrange("m r n -> m (r n)")).then_inc(mask_ready, 1)

            def fold_and_mask(g):
                dve.wait_ge(logits_ready, g + 1)
                for t in range(TB):
                    nc.vector.tensor_reduce(logits[t * N:(t + 1) * N],
                                            raw_logits[t * N:(t + 1) * N].rearrange("p r s n -> p r n s")
                                            [:, :, t * N:(t + 1) * N], AX_X, ALU.add).then_inc(folded, 1)
                dve.wait_ge(folded, 2 * g + 2)
                dve.wait_ge(mask_ready, g + 1)
                nc.vector.scalar_tensor_tensor(out=logits[:], in0=logits[:], scalar=0.0, in1=mask[:],
                                               op0=ALU.max, op1=ALU.mult).then_inc(masked, 1)

            def subtract_max(g):
                dve.wait_ge(masked, g + 1)
                nc.vector.tensor_reduce(neg_max[:], logits[:], AX_X, ALU.max, negate=True).then_inc(max_ready, 1)
                dve.wait_ge(max_ready, g + 1)
                nc.vector.tensor_tensor(logits[:], logits[:], neg_max[:].unsqueeze(2).broadcast_to([P, R, N]),
                                        ALU.add).then_inc(shifted, 1)

            def softmax(g, first):
                dve.wait_ge(exp_ready, g + 1)
                nc.vector.tensor_reduce(total[:], logits[:], AX_X, ALU.add).then_inc(total_ready, 1)
                dve.wait_ge(total_ready, g + 1)
                nc.vector.reciprocal(inverse[:], total[:]).then_inc(inverse_ready, 1)
                if not first:
                    dve.wait_ge(blocks_high, 2 * g)
                dve.wait_ge(inverse_ready, g + 1)
                nc.vector.tensor_tensor(probs[:], logits[:], inverse[:].unsqueeze(2).broadcast_to([P, R, N]),
                                        ALU.mult).then_inc(probs_ready, 1)

            def blocks_part(g):
                dve.wait_ge(probs_ready, g + 1)
                for t in range(TB):
                    dve.wait_ge(blocks_high, 2 * g + t + 1)
                    place = slice(t * N, (t + 1) * N)
                    nc.vector.tensor_tensor(blocks[place, LOW, :, place], probs[place],
                                            blocks[place, HIGH, :, place].bitcast(F32),
                                            ALU.subtract).then_inc(blocks_low, 1)

            dve.wait_ge(x_quads_loaded, 16 * C)
            for h in range(2):
                turn(h, h, x_quads[:])
            for h in range(2):
                turn_low(h, h, xT[:, 0])
            dve.wait_ge(w_high, 1)
            nc.vector.tensor_tensor(w_split[:, :, LOW, :], w_raw, w_split[:, :, HIGH, :].bitcast(F32),
                                    ALU.subtract).then_inc(w_low, 1)
            for n, (src, loaded, dst) in enumerate(SETUP[1:], 1):
                dve.wait_ge(loaded, 16 * C)
                for h in range(2):
                    turn_weight(2 * n + h, h, src)
                for h in range(2):
                    turn_low(2 * n + h, h, dst)
            for r in range(EARLY):
                v_part(0, r)
            for j in range(C):
                m_part(j)
            dve.wait_ge(adj_loaded, 16 * 8)

            def step(g, half, slot, first=False, last=False):
                u = halves_before(g + 1)
                z_part(g, 0)
                if not last:
                    dve.wait_ge(x_quads_loaded, 16 * C * (g + 2))
                    turn(u, 0, x_quads[:])
                z_part(g, 1)
                if not first:
                    dve.wait_ge(stored[1 - slot], 16 * (half + slot))
                    dve.wait_ge(x_loaded[1 - slot], 16 * (half + slot))
                    residual(g - 1, 1 - slot, 0)
                    residual(g - 1, 1 - slot, 1)
                if not last:
                    turn(u + 1, 1, x_quads[:])
                z_part(g, 2)
                if not first:
                    residual(g - 1, 1 - slot, 2)
                    residual(g - 1, 1 - slot, 3)
                    dve.wait_ge(stats_ready, R * g)
                z_part(g, 3)
                if not first:
                    aggregate()
                make_mask(g)
                if not first:
                    v_part(g, 0)
                fold_and_mask(g)
                subtract_max(g)
                if not first:
                    v_part(g, 1)
                softmax(g, first)
                if not first:
                    v_part(g, 2)
                blocks_part(g)
                v_part(g, 3)

            steps(dve, step)
            dve.wait_ge(stored[1], 16 * (G // 2))
            dve.wait_ge(x_loaded[1], 16 * (G // 2))
            for r in range(R):
                residual(G - 1, 1, r)
            dve.wait_ge(stats_ready, R * G)
            aggregate()

        @block.gpsimd
        def _(pool):
            for constant, value in ((eps, EPS), (minus_half, -0.5), (minus_one, -1.0)):
                nc.gpsimd.memset(constant[:], value).then_inc(constants_ready, 1)
            nc.gpsimd.memset(blocks[:].bitcast(F32), 0.0).then_inc(blocks_cleared, 1)
            pool.wait_ge(constants_ready, 3)

            def turn_low(u, h, slot):
                pool.wait_ge(turned_high, u + 1)
                nc.gpsimd.tensor_tensor(xT[:, slot, h * H:(h + 1) * H, LOW, :], halfT[:, h],
                                        xT[:, slot, h * H:(h + 1) * H, HIGH, :].bitcast(F32),
                                        ALU.subtract).then_inc(turned_low, 1)

            def scale_and_shift(g):
                pool.wait_ge(moments_ready, R * g + R)
                nc.gpsimd.tensor_tensor(var_eps[:], moments[:, :, 1], eps[:], ALU.add).then_inc(var_ready, 1)
                pool.wait_ge(var_ready, g + 1)
                pool.wait_ge(v_high, R * g + 1)
                nc.gpsimd.tensor_tensor(rstd[:], var_eps[:], minus_half[:], ALU.pow).then_inc(rstd_ready, 1)
                pool.wait_ge(rstd_ready, g + 1)
                nc.gpsimd.tensor_tensor(mean_rstd[:], moments[:, :, 0], rstd[:], ALU.mult).then_inc(mean_ready, 1)
                pool.wait_ge(mean_ready, g + 1)
                nc.gpsimd.tensor_tensor(shift[:], mean_rstd[:], minus_one[:], ALU.mult).then_inc(shift_ready, 1)

            def step(g, half, slot, first=False, last=False):
                if not last:
                    turn_low(halves_before(g + 1), 0, 1 - slot)
                    turn_low(halves_before(g + 1) + 1, 1, 1 - slot)
                if not first:
                    scale_and_shift(g - 1)

            steps(pool, step)
            scale_and_shift(G - 1)


_INS = ["x", "adj", "L0_gnn_weight", "L0_gnn_wq", "L0_gnn_wk"]


def kernel(**inputs):
    import numpy as _np
    import concourse.bacc as _bacc
    from concourse import mybir as _mybir
    from concourse.bass_utils import run_bass_kernel_spmd as _run

    nc = _bacc.Bacc("TRN2", target_bir_lowering=False, num_devices=1)
    arrays, args = {}, []
    for name in _INS:
        a = _np.ascontiguousarray(inputs[name])
        arrays[f"in_{name}"] = a
        args.append(nc.dram_tensor(f"in_{name}", a.shape, _mybir.dt.from_np(a.dtype), kind="ExternalInput").ap())
    result = nc.dram_tensor("out", inputs["x"].shape, _mybir.dt.from_np(_np.dtype("float32")),
                            kind="ExternalOutput").ap()
    gnn_layer(nc, *args, result)
    return _run(nc, [arrays], core_ids=[0]).results[0]["out"]
```

```python
from contextlib import ExitStack

import concourse.bass as bass
from concourse import mybir

ALU = mybir.AluOpType
ACT = mybir.ActivationFunctionType
AX_X = mybir.AxisListType.X
F32 = mybir.dt.float32
F32R = mybir.dt.float32r
I32 = mybir.dt.int32

P = 128
Q = 32
EPS = 1e-5
HIGH, LOW = 0, 1


def gnn_layer(nc: bass.Bass, x, adj, weight, wq, wk, out):
    B, N, D = x.shape
    C = D // P
    R = 4
    TB = P // N
    GB = R * TB
    ROWS = R * P
    G = B // GB
    H = C // 2
    assert D == 512 and N == 64 and B % (2 * GB) == 0 and ROWS == D and P // Q == C

    x_rows = x.rearrange("(g r b) n d -> g (b n) r d", r=R, b=TB)
    out_rows = out.rearrange("(g r b) n d -> g (b n) r d", r=R, b=TB)
    x_cols = x.rearrange("(g b) (k a) (q f) -> g q a (b k) f", b=GB, a=Q, f=P)
    wq_cols = wq.rearrange("(k a) (q f) -> q a k f", a=Q, f=P)
    wk_cols = wk.rearrange("(k a) (q f) -> q a k f", a=Q, f=P)
    w_rows = weight.rearrange("(q b e) d -> q e b d", q=C, e=Q)
    adj_blocks = adj.rearrange("(r t) (k a) (h c) -> t h k a r c", t=TB, a=Q, c=Q)

    with ExitStack() as ctx:
        def sb(name, shape, dt=F32):
            return ctx.enter_context(nc.sbuf_tensor(name, shape, dt))

        def sem(name):
            return ctx.enter_context(nc.semaphore(name))

        w_split = sb("w_split", [P, C, 2, D], F32R)
        m_split = sb("m_split", [P, C, 2, D], F32R)
        xT = sb("xT", [P, 2, C, 2, ROWS], F32R)
        zT = sb("zT", [P, C, 2, ROWS], F32R)
        v = sb("v", [P, R, 2, D], F32R)
        blocks = sb("blocks", [P, 2, R, P], F32R)
        x_sb = sb("x_sb", [P, 2, R, D])
        x_quads = sb("x_quads", [P, ROWS // Q, P])
        halfT = sb("halfT", [P, 2, H, ROWS])
        y = sb("y", [P, 2, R, D])
        w_raw = x_sb[:, 1]
        wk_quads = y[:, 0].rearrange("p r (s f) -> p (r s) f", f=P)
        wq_quads = y[:, 1].rearrange("p r (s f) -> p (r s) f", f=P)
        wkT, wqT = xT[:, 1], zT[:]
        adj_sb = sb("adj_sb", [P, G * R, N], I32)
        linked = sb("linked", [P, R, N])
        mask = sb("mask", [P, R, N])
        logits = sb("logits", [P, R, N])
        neg_max = sb("neg_max", [P, R])
        total = sb("total", [P, R])
        inverse = sb("inverse", [P, R])
        probs = sb("probs", [P, R, N])
        stats = sb("stats", [P, R, 6])
        moments = sb("moments", [P, R, 2])
        var_eps = sb("var_eps", [P, R])
        rstd = sb("rstd", [P, R])
        mean_rstd = sb("mean_rstd", [P, R])
        shift = sb("shift", [P, R])
        eps = sb("eps", [P, R])
        minus_half = sb("minus_half", [P, R])
        minus_one = sb("minus_one", [P, R])

        product = [ctx.enter_context(nc.psum_tensor(f"product{i}", [P, D], F32)) for i in range(4)]
        raw_logits = ctx.enter_context(nc.psum_tensor("raw_logits", [P, R, 2, P], F32))
        attended = [ctx.enter_context(nc.psum_tensor(f"attended{i}", [P, D], F32)) for i in range(2)]

        x_quads_loaded, wk_loaded, wq_loaded = sem("x_quads_loaded"), sem("wk_loaded"), sem("wq_loaded")
        w_loaded, adj_loaded = sem("w_loaded"), sem("adj_loaded")
        x_loaded = [sem("x_loaded0"), sem("x_loaded1")]
        stored = [sem("stored0"), sem("stored1")]
        blocks_cleared = sem("blocks_cleared")
        constants_ready = sem("constants_ready")
        turned = sem("turned")
        turned_high, turned_low = sem("turned_high"), sem("turned_low")
        w_high, w_low = sem("w_high"), sem("w_low")
        w_low_pool = sem("w_low_pool")
        m_ready, m_high, m_low = sem("m_ready"), sem("m_high"), sem("m_low")
        z_ready, z_high, z_low = sem("z_ready"), sem("z_high"), sem("z_low")
        v_ready, v_high, v_low = sem("v_ready"), sem("v_high"), sem("v_low")
        logits_ready = sem("logits_ready")
        folded = sem("folded")
        compared, mask_ready, masked = sem("compared"), sem("mask_ready"), sem("masked")
        max_ready, shifted = sem("max_ready"), sem("shifted")
        exp_ready, total_ready, inverse_ready = sem("exp_ready"), sem("total_ready"), sem("inverse_ready")
        probs_ready = sem("probs_ready")
        blocks_high, blocks_low = sem("blocks_high"), sem("blocks_low")
        out_ready = sem("out_ready")
        residual_added = sem("residual_added")
        stats_ready, moments_ready = sem("stats_ready"), sem("moments_ready")
        var_ready, rstd_ready, mean_ready = sem("var_ready"), sem("rstd_ready"), sem("mean_ready")
        shift_ready = sem("shift_ready")
        normalised = sem("normalised")

        WEIGHT_HALVES = ((0, wk_quads, wk_loaded, wkT), (0, wq_quads, wq_loaded, wqT),
                         (1, wk_quads, wk_loaded, wkT), (1, wq_quads, wq_loaded, wqT))

        def halves_before(g):
            return len(WEIGHT_HALVES) + 2 * g

        FIRST_TILES = (1, 2, 3, 0)

        m_banks = [raw_logits[:, 0:2].rearrange("p r s n -> p (r s n)"),
                   raw_logits[:, 2:4].rearrange("p r s n -> p (r s n)"), attended[0][:], attended[1][:]]

        def steps(engine, step):
            step(0, 0, 0, first=True)
            with engine.Fori(0, (G - 2) // 2) as i:
                step(2 * i + 1, i, 1)
                step(2 * i + 2, i + 1, 0)
            step(G - 1, (G - 1) // 2, 1, last=True)

        block = ctx.enter_context(nc.Block())

        @block.sync
        def _(sp):
            def load_quads(dst, src, loaded):
                for q in range(C):
                    sp.dma_start(dst[q * Q:(q + 1) * Q], src[q]).then_inc(loaded, 16)

            for slot in range(2):
                sp.sem_inc(stored[slot], 16)
            load_quads(x_quads[:], x_cols[0], x_quads_loaded)
            load_quads(w_raw, w_rows, w_loaded)
            load_quads(wk_quads, wk_cols, wk_loaded)
            load_quads(wq_quads, wq_cols, wq_loaded)
            for t in range(TB):
                for h in range(N // Q):
                    for k in range(N // Q):
                        sp.dma_start(adj_sb[(t * 2 + h) * Q:(t * 2 + h + 1) * Q, :, k * Q:(k + 1) * Q],
                                     adj_blocks[t, h, k]).then_inc(adj_loaded, 16)

            def store(g, slot):
                sp.wait_ge(normalised, R * (g + 1))
                sp.dma_start(out_rows[g], y[:, slot]).then_inc(stored[slot], 16)

            def step(g, half, slot, first=False, last=False):
                if not last:
                    sp.wait_ge(turned, 2 if first else halves_before(g) + 2)
                    load_quads(x_quads[:], x_cols[g + 1], x_quads_loaded)
                if slot == 1 and not first:
                    sp.wait_ge(w_low, H)
                    sp.wait_ge(w_low_pool, C - H)
                sp.dma_start(x_sb[:, slot], x_rows[g]).then_inc(x_loaded[slot], 16)
                if not first:
                    store(g - 1, 1 - slot)

            steps(sp, step)
            for r in range(R):
                sp.wait_ge(normalised, R * (G - 1) + r + 1)
                sp.dma_start(out_rows[G - 1, :, r], y[:, 1, r]).then_inc(stored[1], 16)
            sp.wait_ge(stored[0], 16 * (1 + G // 2))
            sp.wait_ge(stored[1], 16 * (G // 2 + R))

        @block.tensor
        def _(pe):
            def split_product(bank, stationary, moving, chunks=range(C)):
                for c in chunks:
                    for s, t in ((HIGH, HIGH), (HIGH, LOW), (LOW, HIGH)):
                        mm = nc.tensor.matmul(bank, stationary(c, s), moving(c, t),
                                              start=(c == 0 and s == t), stop=(c == C - 1 and s == LOW))
                return mm

            def z_chunk(slot, i):
                split_product(product[i][:], lambda c, s: m_split[:, c, s, i * P:(i + 1) * P],
                              lambda c, s: xT[:, slot, c, s, :]).then_inc(z_ready, 1)

            def v_tile(slot, r):
                split_product(product[r][:], lambda c, s: xT[:, slot, c, s, r * P:(r + 1) * P],
                              lambda c, s: w_split[:, c, s, :]).then_inc(v_ready, 1)

            def logits_of(g, slot):
                pe.wait_ge(z_low, C * g + C)
                for r in range(R):
                    rows = slice(r * P, (r + 1) * P)
                    for c in range(C):
                        nc.tensor.matmul(raw_logits[:, r], zT[:, c, HIGH, rows], xT[:, slot, c, :, rows],
                                         start=(c == 0), stop=False)
                        mm = nc.tensor.matmul(raw_logits[:, r, HIGH], zT[:, c, LOW, rows],
                                              xT[:, slot, c, HIGH, rows], start=False, stop=(c == C - 1))
                mm.then_inc(logits_ready, 1)

            def attend(g, r, tail=False):
                if r == 0 or tail:
                    pe.wait_ge(v_low, R * g + (r + 1 if tail else R))
                if r == 0:
                    pe.wait_ge(blocks_high, 2 * g + 2)
                    pe.wait_ge(blocks_low, 2 * g + 2)
                if r >= 2:
                    pe.wait_ge(residual_added, R * g + r - 1)
                for s, t in ((HIGH, HIGH), (HIGH, LOW), (LOW, HIGH)):
                    mm = nc.tensor.matmul(attended[r % 2][:], blocks[:, s, r, :], v[:, r, t, :],
                                          start=(s == t), stop=(s == LOW))
                mm.then_inc(out_ready, 1)

            r = FIRST_TILES[0]
            for c in range(C):
                pe.wait_ge(turned_low, c // H + 1)
                if c < H:
                    pe.wait_ge(w_low, c + 1)
                else:
                    pe.wait_ge(w_low_pool, c - H + 1)
                mm = split_product(product[r][:], lambda c, s: xT[:, 0, c, s, r * P:(r + 1) * P],
                                   lambda c, s: w_split[:, c, s, :], chunks=[c])
            mm.then_inc(v_ready, 1)
            v_tile(0, FIRST_TILES[1])
            for h in range(2):
                pe.wait_ge(turned_low, 4 + 2 * h)
                for j in range(C):
                    mm = split_product(m_banks[j], lambda c, s: wkT[:, c, s, j * P:(j + 1) * P],
                                       lambda c, s: wqT[:, c, s, :], chunks=range(h * H, (h + 1) * H))
                    if h == 1:
                        mm.then_inc(m_ready, 1)
            v_tile(0, FIRST_TILES[2])
            pe.wait_ge(m_low, C)

            def step(g, half, slot, first=False, last=False):
                if not first:
                    pe.wait_ge(turned_low, halves_before(g) + 2)
                for i in range(C):
                    if not first:
                        pe.wait_ge(v_low, R * g - R + i + 1)
                    elif i > 0:
                        pe.wait_ge(v_low, i)
                    z_chunk(slot, i)
                    if not first and i in (1, 2):
                        attend(g - 1, 2 * i - 2)
                        attend(g - 1, 2 * i - 1)
                for r in range(1 if first else R):
                    pe.wait_ge(z_low, C * g + r + 1)
                    v_tile(slot, r)
                    if r == 0:
                        logits_of(g, slot)
                if first:
                    pe.wait_ge(v_low, R)

            steps(pe, step)
            for r in range(R):
                attend(G - 1, r, tail=True)

        @block.scalar
        def _(act):
            def turn_high(u, s, h, dst):
                act.wait_ge(turned, u + 1)
                nc.scalar.copy(dst[:, h * H:(h + 1) * H, HIGH, :], halfT[:, s]).then_inc(turned_high, 1)

            def w_part(c):
                nc.scalar.copy(w_split[:, c, HIGH, :], w_raw[:, c, :]).then_inc(w_high, 1)

            def m_part(j):
                act.wait_ge(m_ready, j + 1)
                nc.scalar.copy(m_split[:, j, HIGH, :], m_banks[j]).then_inc(m_high, 1)

            def z_part(g, i):
                act.wait_ge(z_ready, C * g + i + 1)
                nc.scalar.copy(zT[:, i, HIGH, :], product[i][:]).then_inc(z_high, 1)

            def v_part(g, r, n=None):
                act.wait_ge(v_ready, R * g + (r if n is None else n) + 1)
                nc.scalar.copy(v[:, r, HIGH, :], product[r][:]).then_inc(v_high, 1)

            def normalise_tile(slot, r):
                nc.scalar.activation(y[:, slot, r, :], y[:, slot, r, :], ACT.Identity, bias=shift[:, r:r + 1],
                                     scale=rstd[:, r:r + 1]).then_inc(normalised, 1)

            def normalise(g, slot):
                act.wait_ge(shift_ready, g + 1)
                for r in range(R):
                    normalise_tile(slot, r)

            turn_high(0, 0, 0, xT[:, 0])
            act.wait_ge(w_loaded, 16 * C)
            w_part(0)
            w_part(1)
            turn_high(1, 1, 1, xT[:, 0])
            for c in range(H, C):
                w_part(c)
            for u, (h, _, _, dst) in enumerate(WEIGHT_HALVES, 2):
                turn_high(u, u % 2, h, dst)
            v_part(0, FIRST_TILES[0], 0)
            v_part(0, FIRST_TILES[1], 1)
            for j in range(C):
                m_part(j)
            v_part(0, FIRST_TILES[2], 2)

            def step(g, half, slot, first=False, last=False):
                if not first:
                    act.wait_ge(logits_ready, g)
                    act.wait_ge(v_ready, R * g)
                for i in range(C):
                    z_part(g, i)
                    if not last and i in (1, 2):
                        turn_high(halves_before(g + 1) + i - 1, i - 1, i - 1, xT[:, 1 - slot])
                if not first:
                    normalise(g - 1, 1 - slot)
                    act.wait_ge(out_ready, R * g)
                    v_part(g, 0)
                    v_part(g, 1)
                else:
                    v_part(g, FIRST_TILES[3], 3)
                act.wait_ge(shifted, g + 1)
                nc.scalar.activation(logits[:], logits[:], ACT.Exp).then_inc(exp_ready, 1)
                if not first:
                    v_part(g, 2)
                else:
                    act.wait_ge(blocks_cleared, 1)
                act.wait_ge(probs_ready, g + 1)
                for t in range(TB):
                    nc.scalar.copy(blocks[t * N:(t + 1) * N, HIGH, :, t * N:(t + 1) * N],
                                   probs[t * N:(t + 1) * N]).then_inc(blocks_high, 1)
                if not first:
                    v_part(g, 3)

            steps(act, step)
            for r in range(R):
                act.wait_ge(shift_ready, G + r)
                normalise_tile(1, r)

        @block.vector
        def _(dve):
            def turn(u, h, src):
                if u >= 2:
                    dve.wait_ge(turned_low, u - 1)
                nc.vector.transpose(halfT[:, h].rearrange("p b (k a) -> p b k a", a=Q),
                                    src.rearrange("p k (b c) -> p b k c", c=Q)[:, h * H:(h + 1) * H]).then_inc(turned, 1)

            def turn_weight(u, s, h, src):
                dve.wait_ge(turned_low, u - 1)
                for b in range(H):
                    last = nc.vector.transpose(halfT[:, s, b].rearrange("p (f q a) -> p q f a", q=C, a=Q),
                                               src.rearrange("p (q f) (b c) -> p b q f c", q=C, c=Q)[:, h * H + b])
                last.then_inc(turned, 1)

            def turn_low(u, s, h, dst):
                dve.wait_ge(turned_high, u + 1)
                dve.wait_ge(turned, u + 1)
                nc.vector.tensor_tensor(dst[:, h * H:(h + 1) * H, LOW, :], halfT[:, s],
                                        dst[:, h * H:(h + 1) * H, HIGH, :].bitcast(F32),
                                        ALU.subtract).then_inc(turned_low, 1)

            def low_part(split, whole):
                return nc.vector.tensor_tensor(split[:, LOW, :], whole, split[:, HIGH, :].bitcast(F32), ALU.subtract)

            def m_part(j):
                dve.wait_ge(m_high, j + 1)
                low_part(m_split[:, j], m_banks[j]).then_inc(m_low, 1)

            def w_part(c):
                dve.wait_ge(w_high, c + 1)
                low_part(w_split[:, c], w_raw[:, c, :]).then_inc(w_low, 1)

            def z_part(g, i):
                dve.wait_ge(z_high, C * g + i + 1)
                low_part(zT[:, i], product[i][:]).then_inc(z_low, 1)

            def v_part(g, r, n=None):
                dve.wait_ge(v_high, R * g + (r if n is None else n) + 1)
                low_part(v[:, r], product[r][:]).then_inc(v_low, 1)

            def add_residual(g, slot, r):
                dve.wait_ge(out_ready, R * g + r + 1)
                nc.vector.tensor_tensor(y[:, slot, r, :], attended[r % 2][:], x_sb[:, slot, r, :],
                                        ALU.add).then_inc(residual_added, 1)

            def take_stats(g, slot, r):
                dve.wait_ge(residual_added, R * g + r + 1)
                nc.vector.bn_stats(stats[:, r, :], y[:, slot, r, :]).then_inc(stats_ready, 1)

            def residual_pair(g, slot, r):
                for tile in (r, r + 1):
                    add_residual(g, slot, tile)
                for tile in (r, r + 1):
                    take_stats(g, slot, tile)

            def aggregate(tiles):
                for r in tiles:
                    nc.vector.bn_aggr(moments[:, r, :], stats[:, r, :]).then_inc(moments_ready, 1)

            def make_mask(g):
                nc.vector.tensor_scalar(linked[:], adj_sb[:, bass.ts(g, R)], 0.0, None,
                                        ALU.not_equal).then_inc(compared, 1)
                dve.wait_ge(compared, g + 1)
                nc.vector.transpose(mask[:].rearrange("m r n -> m (r n)"),
                                    linked[:].rearrange("m r n -> m (r n)")).then_inc(mask_ready, 1)

            def fold_and_mask(g):
                dve.wait_ge(logits_ready, g + 1)
                for t in range(TB):
                    nc.vector.tensor_reduce(logits[t * N:(t + 1) * N],
                                            raw_logits[t * N:(t + 1) * N].rearrange("p r s n -> p r n s")
                                            [:, :, t * N:(t + 1) * N], AX_X, ALU.add).then_inc(folded, 1)
                dve.wait_ge(folded, 2 * g + 2)
                dve.wait_ge(mask_ready, g + 1)
                nc.vector.scalar_tensor_tensor(out=logits[:], in0=logits[:], scalar=0.0, in1=mask[:],
                                               op0=ALU.max, op1=ALU.mult).then_inc(masked, 1)

            def subtract_max(g):
                dve.wait_ge(masked, g + 1)
                nc.vector.tensor_reduce(neg_max[:], logits[:], AX_X, ALU.max, negate=True).then_inc(max_ready, 1)
                dve.wait_ge(max_ready, g + 1)
                nc.vector.tensor_tensor(logits[:], logits[:], neg_max[:].unsqueeze(2).broadcast_to([P, R, N]),
                                        ALU.add).then_inc(shifted, 1)

            def softmax(g, first):
                dve.wait_ge(exp_ready, g + 1)
                nc.vector.tensor_reduce(total[:], logits[:], AX_X, ALU.add).then_inc(total_ready, 1)
                dve.wait_ge(total_ready, g + 1)
                nc.vector.reciprocal(inverse[:], total[:]).then_inc(inverse_ready, 1)
                if not first:
                    dve.wait_ge(blocks_high, 2 * g)
                dve.wait_ge(inverse_ready, g + 1)
                nc.vector.tensor_tensor(probs[:], logits[:], inverse[:].unsqueeze(2).broadcast_to([P, R, N]),
                                        ALU.mult).then_inc(probs_ready, 1)

            def blocks_part(g):
                dve.wait_ge(probs_ready, g + 1)
                for t in range(TB):
                    dve.wait_ge(blocks_high, 2 * g + t + 1)
                    place = slice(t * N, (t + 1) * N)
                    nc.vector.tensor_tensor(blocks[place, LOW, :, place], probs[place],
                                            blocks[place, HIGH, :, place].bitcast(F32),
                                            ALU.subtract).then_inc(blocks_low, 1)

            dve.wait_ge(x_quads_loaded, 16 * C)
            for h in range(2):
                turn(h, h, x_quads[:])
            turn_low(0, 0, 0, xT[:, 0])
            for c in range(H):
                w_part(c)
            turn_low(1, 1, 1, xT[:, 0])
            for h in range(2):
                pair = list(enumerate(WEIGHT_HALVES, 2))[2 * h:2 * h + 2]
                for u, (_, src, loaded, _) in pair:
                    dve.wait_ge(loaded, 16 * C)
                    turn_weight(u, u % 2, h, src)
                for u, (_, _, _, dst) in pair:
                    turn_low(u, u % 2, h, dst)
            v_part(0, FIRST_TILES[0], 0)
            v_part(0, FIRST_TILES[1], 1)
            for j in range(C):
                m_part(j)
            v_part(0, FIRST_TILES[2], 2)
            dve.wait_ge(adj_loaded, 16 * 8)

            def step(g, half, slot, first=False, last=False):
                u = halves_before(g + 1)
                z_part(g, 0)
                if not last:
                    dve.wait_ge(x_quads_loaded, 16 * C * (g + 2))
                    turn(u, 0, x_quads[:])
                z_part(g, 1)
                if not first:
                    dve.wait_ge(stored[1 - slot], 16 * (half + slot))
                    dve.wait_ge(x_loaded[1 - slot], 16 * (half + slot))
                    residual_pair(g - 1, 1 - slot, 0)
                if not last:
                    turn(u + 1, 1, x_quads[:])
                z_part(g, 2)
                if not first:
                    residual_pair(g - 1, 1 - slot, 2)
                    dve.wait_ge(stats_ready, R * g)
                z_part(g, 3)
                if not first:
                    aggregate(range(R))
                make_mask(g)
                if first:
                    v_part(g, FIRST_TILES[3], 3)
                else:
                    v_part(g, 0)
                fold_and_mask(g)
                subtract_max(g)
                if not first:
                    v_part(g, 1)
                softmax(g, first)
                if not first:
                    v_part(g, 2)
                blocks_part(g)
                if not first:
                    v_part(g, 3)

            steps(dve, step)
            dve.wait_ge(stored[1], 16 * (G // 2))
            dve.wait_ge(x_loaded[1], 16 * (G // 2))
            add_residual(G - 1, 1, 0)
            for r in range(R):
                if r > 0:
                    dve.wait_ge(stats_ready, R * (G - 1) + r)
                    aggregate([r - 1])
                take_stats(G - 1, 1, r)
                if r + 1 < R:
                    add_residual(G - 1, 1, r + 1)
            dve.wait_ge(stats_ready, R * G)
            aggregate([R - 1])

        @block.gpsimd
        def _(pool):
            for constant, value in ((eps, EPS), (minus_half, -0.5), (minus_one, -1.0)):
                nc.gpsimd.memset(constant[:], value).then_inc(constants_ready, 1)
            nc.gpsimd.memset(blocks[:].bitcast(F32), 0.0).then_inc(blocks_cleared, 1)
            pool.wait_ge(constants_ready, 3)

            for c in range(H, C):
                pool.wait_ge(w_high, c + 1)
                nc.gpsimd.tensor_tensor(w_split[:, c, LOW, :], w_raw[:, c, :], w_split[:, c, HIGH, :].bitcast(F32),
                                        ALU.subtract).then_inc(w_low_pool, 1)

            def turn_low(u, h, slot):
                pool.wait_ge(turned_high, u + 1)
                nc.gpsimd.tensor_tensor(xT[:, slot, h * H:(h + 1) * H, LOW, :], halfT[:, h],
                                        xT[:, slot, h * H:(h + 1) * H, HIGH, :].bitcast(F32),
                                        ALU.subtract).then_inc(turned_low, 1)

            def scale_and_shift(n, tiles):
                nc.gpsimd.tensor_tensor(var_eps[:, tiles], moments[:, tiles, 1], eps[:, tiles],
                                        ALU.add).then_inc(var_ready, 1)
                pool.wait_ge(var_ready, n)
                nc.gpsimd.tensor_tensor(rstd[:, tiles], var_eps[:, tiles], minus_half[:, tiles],
                                        ALU.pow).then_inc(rstd_ready, 1)
                pool.wait_ge(rstd_ready, n)
                nc.gpsimd.tensor_tensor(mean_rstd[:, tiles], moments[:, tiles, 0], rstd[:, tiles],
                                        ALU.mult).then_inc(mean_ready, 1)
                pool.wait_ge(mean_ready, n)
                nc.gpsimd.tensor_tensor(shift[:, tiles], mean_rstd[:, tiles], minus_one[:, tiles],
                                        ALU.mult).then_inc(shift_ready, 1)

            def step(g, half, slot, first=False, last=False):
                if not last:
                    turn_low(halves_before(g + 1), 0, 1 - slot)
                    turn_low(halves_before(g + 1) + 1, 1, 1 - slot)
                if not first:
                    pool.wait_ge(moments_ready, R * g)
                    pool.wait_ge(v_high, R * g - R + 1)
                    scale_and_shift(g, slice(0, R))

            steps(pool, step)
            for r in range(R):
                pool.wait_ge(moments_ready, R * (G - 1) + r + 1)
                if r == 0:
                    pool.wait_ge(v_high, R * (G - 1) + 1)
                scale_and_shift(G + r, slice(r, r + 1))


_INS = ["x", "adj", "L0_gnn_weight", "L0_gnn_wq", "L0_gnn_wk"]


def kernel(**inputs):
    import numpy as _np
    import concourse.bacc as _bacc
    from concourse import mybir as _mybir
    from concourse.bass_utils import run_bass_kernel_spmd as _run

    nc = _bacc.Bacc("TRN2", target_bir_lowering=False, num_devices=1)
    arrays, args = {}, []
    for name in _INS:
        a = _np.ascontiguousarray(inputs[name])
        arrays[f"in_{name}"] = a
        args.append(nc.dram_tensor(f"in_{name}", a.shape, _mybir.dt.from_np(a.dtype), kind="ExternalInput").ap())
    result = nc.dram_tensor("out", inputs["x"].shape, _mybir.dt.from_np(_np.dtype("float32")),
                            kind="ExternalOutput").ap()
    gnn_layer(nc, *args, result)
    return _run(nc, [arrays], core_ids=[0]).results[0]["out"]
```
